# Optimizing a Trainium2 kernel written in Bass

```python
import numpy as np
import jax
import jax.numpy as jnp

def _softmax(x, axis=-1):
    return jax.nn.softmax(x, axis=axis)

def _gelu(x):
    return jax.nn.gelu(x, approximate=True)

def _silu(x):
    return jax.nn.silu(x)

def _sigmoid(x):
    return jax.nn.sigmoid(x)

def _layernorm(x, axis=-1, eps=1e-05):
    m = jnp.mean(x, axis=axis, keepdims=True)
    v = jnp.var(x, axis=axis, keepdims=True)
    return (x - m) / jnp.sqrt(v + eps)

def _scatter_add(tgt, idx, src, axis=0):
    return tgt.at[idx].add(src)

def _segment_sum(src, seg, n):
    return jax.ops.segment_sum(src, seg, n)
kernel_name = 'mk_adj_preln_d2_adj_r2_fd6dc4'

def setup_inputs(seed: int=0):
    np.random.seed(seed)
    _w = jnp.asarray

    def _rec_inputs():
        import jax
        import jax.numpy as jnp
        _gk = jax.random.key(seed)
        x = -0.0002928 + 1 * jax.random.normal(jax.random.fold_in(_gk, 1), (8, 1024, 256), jnp.float32)
        _w = (1.0 + jnp.arange(1024, dtype=jnp.float32)) ** (-0.5)
        _w = _w / _w.mean()
        _pij = jnp.clip(0.015625 * _w[:, None] * _w[None, :], 0.0, 1.0)
        _a = jax.random.uniform(jax.random.fold_in(_gk, 2), (8, 1024, 1024)) < _pij
        adj = _a.astype(jnp.int32)
        return (x, adj)
    x, adj = _rec_inputs()

    def _L0_gnn_setup():
        import jax, jax.numpy as jnp
        import numpy as np
        L = 3
        D = 256
        B, N = (8, 512)
        EPS = 1e-05

        def layernorm(x, gamma, beta):
            mu = jnp.mean(x, axis=-1, keepdims=True)
            var = jnp.var(x, axis=-1, keepdims=True)
            return (x - mu) * jax.lax.rsqrt(var + EPS) * gamma + beta
        key = jax.random.key(seed)
        ks = jax.random.split(key, 12)
        s = 1.0 / np.sqrt(D)
        node_features = jax.random.normal(ks[0], (B, N, D), dtype=jnp.float32)
        adjacency_matrix = jax.random.randint(ks[1], (B, N, N), 0, 2, dtype=jnp.int32)
        return {'node_features': node_features, 'adjacency_matrix': adjacency_matrix, 'attn_w': jax.random.normal(ks[2], (L, 2 * D), dtype=jnp.float32) * (1.0 / np.sqrt(2 * D)), 'attn_b': jax.random.normal(ks[3], (L,), dtype=jnp.float32) * 0.01, 'W1': jax.random.normal(ks[4], (L, D, 4 * D), dtype=jnp.float32) * s, 'b1': jnp.zeros((L, 4 * D), dtype=jnp.float32), 'W2': jax.random.normal(ks[5], (L, 4 * D, D), dtype=jnp.float32) * (1.0 / np.sqrt(4 * D)), 'b2': jnp.zeros((L, D), dtype=jnp.float32), 'g1': jnp.ones((L, D), dtype=jnp.float32), 'beta1': jnp.zeros((L, D), dtype=jnp.float32), 'g2': jnp.ones((L, D), dtype=jnp.float32), 'beta2': jnp.zeros((L, D), dtype=jnp.float32)}
    _L0_gnn_all = _L0_gnn_setup()
    _L0_gnn_in = {k: v for k, v in _L0_gnn_all.items() if k in ('attn_w', 'attn_b', 'W1', 'b1', 'W2', 'b2', 'g1', 'beta1', 'g2', 'beta2')}
    del _L0_gnn_all

    def _L1_gnn_setup():
        import jax, jax.numpy as jnp
        import numpy as np
        ALPHA = 0.2
        MASK_VAL = -1000000000.0
        key = jax.random.key(seed)
        k1, k2, k3, k4 = jax.random.split(key, 4)
        B, N, F_in, F_out = (8, 1024, 256, 256)
        h = jax.random.normal(k1, (B, N, F_in), dtype=jnp.float32)
        adj = jax.random.randint(k2, (B, N, N), 0, 2, dtype=jnp.int32)

        def xavier(k, shape, gain=1.414):
            fan_in, fan_out = (shape[0], shape[1])
            bound = gain * np.sqrt(6.0 / (fan_in + fan_out))
            return jax.random.uniform(k, shape, jnp.float32, -bound, bound)
        W = xavier(k3, (F_in, F_out))
        a = xavier(k4, (2 * F_out, 1))
        return {'h': h, 'adj': adj, 'W': W, 'a': a}
    _L1_gnn_all = _L1_gnn_setup()
    _L1_gnn_in = {k: v for k, v in _L1_gnn_all.items() if k in ('W', 'a')}
    del _L1_gnn_all
    return {'x': x, 'adj': adj, 'L0_gnn_attn_w': _L0_gnn_in['attn_w'], 'L0_gnn_attn_b': _L0_gnn_in['attn_b'], 'L0_gnn_W1': _L0_gnn_in['W1'], 'L0_gnn_b1': _L0_gnn_in['b1'], 'L0_gnn_W2': _L0_gnn_in['W2'], 'L0_gnn_b2': _L0_gnn_in['b2'], 'L0_gnn_g1': _L0_gnn_in['g1'], 'L0_gnn_beta1': _L0_gnn_in['beta1'], 'L0_gnn_g2': _L0_gnn_in['g2'], 'L0_gnn_beta2': _L0_gnn_in['beta2'], 'L1_gnn_W': _L1_gnn_in['W'], 'L1_gnn_a': _L1_gnn_in['a']}

def reference(x, adj, L0_gnn_attn_w, L0_gnn_attn_b, L0_gnn_W1, L0_gnn_b1, L0_gnn_W2, L0_gnn_b2, L0_gnn_g1, L0_gnn_beta1, L0_gnn_g2, L0_gnn_beta2, L1_gnn_W, L1_gnn_a):
    import jax
    import jax.numpy as jnp

    def _L0_gnn_ref(node_features, adjacency_matrix, attn_w, attn_b, W1, b1, W2, b2, g1, beta1, g2, beta2):
        import jax, jax.numpy as jnp
        import numpy as np
        L = 3
        D = 256
        B, N = (8, 512)
        EPS = 1e-05

        def layernorm(x, gamma, beta):
            mu = jnp.mean(x, axis=-1, keepdims=True)
            var = jnp.var(x, axis=-1, keepdims=True)
            return (x - mu) * jax.lax.rsqrt(var + EPS) * gamma + beta
        n = adjacency_matrix.shape[-1]
        mask = adjacency_matrix.astype(jnp.float32) + jnp.eye(n, dtype=jnp.float32) > 0
        x = node_features
        d = x.shape[-1]
        for l in range(attn_w.shape[0]):
            si = x @ attn_w[l, :d]
            sj = x @ attn_w[l, d:]
            scores = si[:, :, None] + sj[:, None, :] + attn_b[l]
            scores = jnp.where(scores >= 0, scores, 0.2 * scores)
            scores = jnp.where(mask, scores, -jnp.inf)
            attn = jax.nn.softmax(scores, axis=-1)
            agg = jnp.einsum('bij,bjd->bid', attn, x)
            h = layernorm(x + agg, g1[l], beta1[l])
            ff = jax.nn.gelu(h @ W1[l] + b1[l], approximate=False) @ W2[l] + b2[l]
            x = layernorm(h + ff, g2[l], beta2[l])
        return x

    def _L1_gnn_ref(h, adj, W, a):
        import jax, jax.numpy as jnp
        import numpy as np
        ALPHA = 0.2
        MASK_VAL = -1000000000.0
        Fout = W.shape[1]
        Wh = jnp.matmul(h, W)
        a1 = a[:Fout, 0]
        a2 = a[Fout:, 0]
        e_i = jnp.einsum('bnf,f->bn', Wh, a1)
        e_j = jnp.einsum('bnf,f->bn', Wh, a2)
        e = e_i[:, :, None] + e_j[:, None, :]
        e = jax.nn.leaky_relu(e, negative_slope=ALPHA)
        e = jnp.where(adj == 0, MASK_VAL, e)
        attention = jax.nn.softmax(e, axis=2)
        h_prime = jnp.matmul(attention, Wh)
        return jax.nn.elu(h_prime)
    h = jnp.maximum(_layernorm(x, axis=-1), 0.0)
    x = x + _L0_gnn_ref(h, adj, L0_gnn_attn_w, L0_gnn_attn_b, L0_gnn_W1, L0_gnn_b1, L0_gnn_W2, L0_gnn_b2, L0_gnn_g1, L0_gnn_beta1, L0_gnn_g2, L0_gnn_beta2)
    h = jnp.maximum(_layernorm(x, axis=-1), 0.0)
    x = x + _L1_gnn_ref(h, adj, L1_gnn_W, L1_gnn_a)
    return x

_drawn_inputs = setup_inputs


def setup_inputs(seed=0):
    import zlib

    import numpy as np

    out = dict(_drawn_inputs(seed))
    spreads = {'L0_gnn_b1': (0.0, 0.1),
     'L0_gnn_b2': (0.0, 0.1),
     'L0_gnn_g1': (1.0, 0.2),
     'L0_gnn_beta1': (0.0, 0.1),
     'L0_gnn_g2': (1.0, 0.2),
     'L0_gnn_beta2': (0.0, 0.1)}
    factors = {'L0_gnn_attn_b': 64.0}
    for name, (base, spread) in spreads.items():
        noise = np.random.default_rng([zlib.crc32(name.encode()), seed]).standard_normal(out[name].shape)
        drawn = base * np.exp(spread * noise) if base else spread * noise
        out[name] = jnp.asarray(drawn.astype(out[name].dtype))
    for name, factor in factors.items():
        out[name] = (out[name] * factor).astype(out[name].dtype)
    return out
```

```python
import math
from contextlib import ExitStack

import concourse.bass as bass
from concourse import mybir

P = 128
BATCH, N, D = 8, 1024, 256
LAYERS, FF = 3, 1024
NT = N // P
KD = D // P
FT = FF // P
HALF = N // 2
HT = NT // 2
PAIRS = BATCH // 2
EPS = 1e-5
SLOPE = 0.2
NOEDGE = -1e30
P_LOG = math.log(1024.0)
W_SCALE = 64.0
XRING = 3
START = "start"
AHEAD = 3
CREDIT = 2


def layer_of(q):
    return (q % 8) // 2


def build(nc, x, adj, attn_w, attn_b, W1, b1, W2, b2, g1, beta1, g2, beta2, gatW, gata, out):
    f32, f16, bf16, i32 = mybir.dt.float32, mybir.dt.float16, mybir.dt.bfloat16, mybir.dt.int32
    ALU, ACT = mybir.AluOpType, mybir.ActivationFunctionType

    x_v = x.rearrange("b (t p) d -> b p t d", p=P)
    out_v = out.rearrange("b (t p) d -> b p t d", p=P)
    adj_v = adj.rearrange("b (t p) n -> b p t n", p=P)
    w_scratch = nc.dram_tensor("w_scratch", (LAYERS, P, 4 * 2048), f16).ap()

    ctx = ExitStack()
    with ctx:
        def sb(name, shape, dt=f32):
            return ctx.enter_context(nc.sbuf_tensor(name, shape, dt))

        def ps(name, shape, dt=f32):
            return ctx.enter_context(nc.psum_tensor(name, shape, dt))

        def sem(name):
            return ctx.enter_context(nc.semaphore(name))

        xc = sb("xc", [P, 2, NT, D])
        xh = sb("xh", [P, 2, NT, D + 2], f16)
        xl = sb("xl", [P, 2, NT, D], f16)
        nm = sb("nm", [P, 2, NT, N], bf16)
        nmT = sb("nmT", [P, 2, NT, N], bf16)
        pH = sb("pH", [P, NT, N], f16)
        pL = sb("pL", [P, NT, N], f16)
        wb = sb("wb", [P, 4, 2048], f16)
        hTh = sb("hTh", [P, KD, HALF], f16)
        hTl = sb("hTl", [P, KD, HALF], f16)
        gT = sb("gT", [P, 2, FT, HALF], f16)
        g32 = sb("g32", [P, 2, HALF])
        xs = sb("xs", [P, XRING, HALF])
        r2s = sb("r2s", [P, N])
        adjst = sb("adjst", [P, 2, N], i32)
        gb1 = sb("gb1", [P, 2, D])
        gb2 = sb("gb2", [P, 2, D])
        aw = sb("aw", [P, 2, 2, D])
        ab = sb("ab", [P, LAYERS])
        b1c = sb("b1c", [P, LAYERS, FT])
        b2r = sb("b2r", [P, LAYERS, D], bf16)
        ones3 = sb("ones3", [P, P], bf16)
        onesf = sb("onesf", [P, P], f16)
        gw = sb("gw", [P, 2, KD, D], f16)
        ident = sb("ident", [P, P])
        identb = sb("identb", [P, P], bf16)
        notib = sb("notib", [P, P], bf16)
        sel = sb("sel", [64, NT, P], bf16)
        cT = sb("cT", [64, P], bf16)
        c3 = sb("c3", [P, 2, 4, NT], bf16)
        cr = sb("cr", [P, 2, NT])
        R = sb("R", [P, 2, NT])
        s1 = sb("s1", [P, NT])
        um = sb("um", [P, 2, NT])
        M = sb("M", [P, NT])
        sc = sb("sc", [P, 2, 2, NT])
        sj8 = sb("sj8", [P, NT])
        sj2 = sb("sj2", [P, NT])
        ef = sb("ef", [P, 2, NT])
        ne = sb("ne", [P, NT])
        csum = sb("csum", [P, 2, D])
        junk = sb("junk", [P, 2, D], bf16)
        den = sb("den", [P, NT])
        rden = sb("rden", [P, NT])
        mhalf = sb("mhalf", [P, 1])
        st = sb("st", [P, 3, NT, 6])
        mv = sb("mv", [P, 3, NT, 2])
        ve = sb("ve", [P, 3, NT])
        rs = sb("rs", [P, 3, NT])
        nb = sb("nb", [P, 3, NT])
        xr = adjst[:, 1, 0:2 * D].bitcast(f32).rearrange("p (r d) -> p r d", r=2)
        adjd = adjst[:, 0, :].rearrange("p (t n) -> p t n", t=NT)
        b1rows = xs[0:LAYERS * FT, 2, HALF - P:HALF]
        wv = adjst[:, 1, 2 * D:4 * D].bitcast(f32).rearrange("p (r d) -> p r d", r=2)
        gfree = gT[:, :, :, :].rearrange("p a f n -> p (a f n)")

        def idle(i):
            return gfree[:, i * 4 * D:(i + 1) * 4 * D].bitcast(f32).rearrange("p (r d) -> p r d", r=2)

        xg = idle(0)
        xgT = gfree[:, 4 * D:8 * D].rearrange("p (a k n) -> p a k n", a=2, k=KD)
        v2, vn, va = idle(2), idle(3), idle(4)

        OB = [ps(f"OB{i}", [P, 512]) for i in range(2)]
        FB = [ps(f"FB{i}", [P, 512]) for i in range(2)]
        RB = ps("RB", [P, N])
        TH = ps("TH", [P, KD, 2 * P])
        TP = ps("TP", [P, KD, 2 * P])
        TPb = TP[:, :, :].rearrange("p a b -> p (a b)").bitcast(bf16)
        TPf = TP[:, :, :].rearrange("p a b -> p (a b)")

        const_ready = sem("const_ready")
        aw_ready = [sem(f"aw_ready{i}") for i in range(2)]
        raw_ready = sem("raw_ready")
        w_split = sem("w_split")
        w_stored = sem("w_stored")
        w_ready = sem("w_ready")
        gb1_ready = sem("gb1_ready")
        gb2_ready = sem("gb2_ready")
        x0_ready = sem("x0_ready")
        adj_ready = [sem(f"adj_ready{i}") for i in range(2)]
        diag_ready = sem("diag_ready")
        xr_ready = [sem(f"xr_ready{i}") for i in range(2)]
        out_done = sem("out_done")
        agg_done = sem("agg_done")
        ht_done = sem("ht_done")
        f1_done = sem("f1_done")
        f2_done = sem("f2_done")
        ct_done = sem("ct_done")
        row_done = sem("row_done")
        mt_done = sem("mt_done")
        gt_done = sem("gt_done")
        pt_done = sem("pt_done")
        wh_done = sem("wh_done")
        cs_done = sem("cs_done")
        norm_done = [sem(f"norm_done{i}") for i in range(3)]
        hth_done = sem("hth_done")
        gelu_done = sem("gelu_done")
        ghi_done = sem("ghi_done")
        exp_done = sem("exp_done")
        phi_done = sem("phi_done")
        xh_done = sem("xh_done")
        r2_done = sem("r2_done")
        nmt_done = sem("nmt_done")
        gdt_done = sem("gdt_done")
        pth_done = sem("pth_done")
        wv_done = sem("wv_done")
        elu_exp = sem("elu_exp")
        rden_done = sem("rden_done")
        rden_done_g = sem("rden_done_g")
        den_done = sem("den_done")
        w_zero = sem("w_zero")
        b2_step = sem("b2_step")
        b1t_done = sem("b1t_done")
        ob_free = sem("ob_free")
        bs_done = [sem(f"bs_done{i}") for i in range(3)]
        st_done = [sem(f"st_done{i}") for i in range(3)]
        htl_done = sem("htl_done")
        glo_done = sem("glo_done")
        max_done = sem("max_done")
        col_step = sem("col_step")
        gcol_step = sem("gcol_step")
        c3_done = sem("c3_done")
        cT_done = sem("cT_done")
        x_done = sem("x_done")
        plo_done = sem("plo_done")
        si_done = sem("si_done")
        sc_done = sem("sc_done")
        nm_done = sem("nm_done")
        gd_done = sem("gd_done")
        ptl_done = sem("ptl_done")
        csc_done = sem("csc_done")
        elu_min = sem("elu_min")
        elu_max = sem("elu_max")
        elu_sum = sem("elu_sum")
        eps_done = [sem(f"eps_done{i}") for i in range(3)]
        pow_done = [sem(f"pow_done{i}") for i in range(3)]
        nb_done = [sem(f"nb_done{i}") for i in range(3)]
        mul_done = [sem(f"mul_done{i}") for i in range(2)]
        aff_done = [sem(f"aff_done{i}") for i in range(2)]
        dfix_done = sem("dfix_done")
        xm_done = sem("xm_done")
        xl_done = sem("xl_done")
        x1_done = sem("x1_done")
        o_ready = sem("o_ready")

        def at(p, per_pair, local):
            return local - per_pair if p is START else local

        RAW = {1: 1, 6: 2, 7: 3, 8: 4}
        FIRST = {1: 1, 8: 2}

        def user(k):
            return 16 * k if k <= 6 else 16 * 6 + 8

        USERS = 16 * 6 + 16
        LN1, LN2, LNP = range(3)

        def ln_at(kind, k, t):
            return (32, 8 * RAW[k] + t) if kind == LNP else (48, 8 * k + t)

        counts = [(s, n) for n, sems in [
            (2, [gt_done, cs_done, gd_done, csc_done]),
            (6, [gcol_step]),
            (8, [pt_done, wh_done, r2_done, pth_done, wv_done, ptl_done]),
            (16, [ct_done, mt_done, nmt_done, gdt_done, elu_exp, rden_done_g, den_done, c3_done,
                  cT_done, nm_done, elu_min, elu_max, elu_sum, dfix_done, x1_done, o_ready]),
            (24, [ht_done, row_done, hth_done, htl_done]),
            (32, [*aw_ready, x0_ready, norm_done[2], bs_done[2], st_done[2], eps_done[2],
                  pow_done[2], nb_done[2]]),
            (48, [w_ready, f2_done, *norm_done[0:2], rden_done, *bs_done[0:2], *st_done[0:2],
                  *eps_done[0:2], *pow_done[0:2], *nb_done[0:2], *mul_done, *aff_done]),
            (64, [agg_done, xh_done, max_done, si_done, sc_done, xl_done]),
            (96, [gb1_ready, gb2_ready, f1_done, gelu_done, ghi_done, glo_done]),
            (104, [col_step]),
            (112, [ob_free]),
            (128, [*adj_ready, *xr_ready, exp_done, phi_done, x_done, plo_done, xm_done]),
            (256, [diag_ready, out_done]),
        ] for s in sems]

        arrived = sem("arrived")
        go = {e: sem(f"go_{e}") for e in ("pe", "act", "dve", "pool")}

        def pair_end(eng, name):
            eng.drain().then_inc(arrived, 1)
            eng.wait_ge(go[name], 1)
            eng.sem_inc(go[name], -1)

        block = ctx.enter_context(nc.Block())

        @block.sync
        def _(sp):
            raws = [pL[:, :, :].bitcast(f32), pH[:, :, :].bitcast(f32),
                    nmT[:, 1, :, :].bitcast(f32)]

            def load_graph(slot, b):
                sp.dma_start(xc[:, slot, :, :], x_v[b]).then_inc(x0_ready, 16)

            def load_adj(p, q, b):
                a = FIRST[q]
                for t in range(NT):
                    sp.wait_ge(nm_done, 8 * a + t - 1)
                    sp.dma_start(adjst[:, t % 2, :], adj_v[b][:, t, :]).then_inc(adj_ready[t % 2], 16)

            def load_aw(l):
                w = attn_w[l] if l < LAYERS else gata.rearrange("d o -> (d o)")
                sp.dma_start(aw[:, l % 2, :, :].rearrange("p a d -> p (a d)"),
                             w.partition_broadcast(P)).then_inc(aw_ready[l % 2], 16)

            def next_aw(p, q, l):
                sp.wait_ge(sc_done, 8 * q + 8)
                load_aw(l)

            load_graph(0, 0)
            sp.dma_start(adjst[:, 0, :], adj_v[0][:, 0, :]).then_inc(adj_ready[0], 16)
            sp.dma_start(adjst[:, 1, :], adj_v[0][:, 1, :]).then_inc(adj_ready[1], 16)
            load_aw(0)
            load_aw(1)
            sp.dma_start(ab[:, :], attn_b.partition_broadcast(P)).then_inc(raw_ready, 16)
            sp.dma_start(b1rows, b1.rearrange("l (f p) -> (l f) p", p=P)).then_inc(raw_ready, 16)
            sp.dma_start(r2s[:, 0:LAYERS * D], b2.rearrange("l d -> (l d)").partition_broadcast(P))\
                .then_inc(raw_ready, 16)
            sp.dma_start(g32[:, 0, :].rearrange("p (k d) -> p k d", k=KD),
                         gatW.rearrange("(k p) d -> p k d", p=P)).then_inc(raw_ready, 16)
            for t in range(2, NT):
                sp.wait_ge(nm_done, at(START, 16, 16 + t - 1))
                sp.dma_start(adjst[:, t % 2, :], adj_v[0][:, t, :]).then_inc(adj_ready[t % 2], 16)
            for l in range(LAYERS):
                raw = raws[l].rearrange("p a b -> p (a b)")
                sp.dma_start(raw[:, 0:2048].rearrange("p (k f) -> p k f", k=KD),
                             W1[l].rearrange("(k p) f -> p k f", p=P)).then_inc(raw_ready, 16)
                sp.dma_start(raw[:, 2048:4096].rearrange("p (f d) -> p f d", f=FT),
                             W2[l].rearrange("(f p) d -> p f d", p=P)).then_inc(raw_ready, 16)

            def load_gb(gb, g, beta, l, s):
                sp.dma_start(gb[:, 0, :], g[l].partition_broadcast(P)).then_inc(s, 16)
                sp.dma_start(gb[:, 1, :], beta[l].partition_broadcast(P)).then_inc(s, 16)

            load_gb(gb1, g1, beta1, 0, gb1_ready)
            load_gb(gb2, g2, beta2, 0, gb2_ready)
            stores = [wb[:, :, :].rearrange("p a b -> p (a b)"),
                      gT[:, :, :, :].rearrange("p a f n -> p (a f n)"),
                      nm[:, 1, :, :].rearrange("p t n -> p (t n)").bitcast(f16)]
            for l in range(LAYERS):
                sp.wait_ge(w_split, 2 * (l + 1))
                sp.dma_start(w_scratch[l], stores[l]).then_inc(w_stored, 16)

            def next_layer(p, k, l):
                sp.wait_ge(aff_done[0], 8 * k + 8)
                load_gb(gb1, g1, beta1, l, gb1_ready)
                sp.wait_ge(f2_done, 8 * k + 8)
                sp.dma_start(wb[:, :, :].rearrange("p a b -> p (a b)"), w_scratch[l])\
                    .then_inc(w_ready, 16)
                sp.wait_ge(aff_done[1], 8 * k + 8)
                load_gb(gb2, g2, beta2, l, gb2_ready)

            def load_diagonals(p, b):
                for t in range(NT):
                    sp.dma_start(adjd[:, t, :], adj_v[b][:, t, t * P:(t + 1) * P]).then_inc(diag_ready, 16)

            def load_residual(p, q, b, tiles):
                for t in tiles:
                    if t >= 2:
                        sp.wait_ge(x1_done, 8 * (q - 6) + t - 1)
                    sp.dma_start(xr[:, t % 2, :], x_v[b][:, t, :]).then_inc(xr_ready[t % 2], 16)

            def store_out(p, k, b):
                for t in range(NT):
                    sp.wait_ge(o_ready, 8 * (k - 6) + t + 1)
                    sp.dma_start(out_v[b][:, t, :], xc[:, k % 2, t, :]).then_inc(out_done, 16)

            sp.wait_ge(w_stored, 16 * LAYERS)
            with sp.Fori(0, PAIRS) as p:
                b0 = 2 * p
                b1_ = 2 * p + 1
                bn = (2 * p + 2) % BATCH
                load_graph(1, b1_)
                load_adj(p, 1, b1_)
                next_aw(p, 1, 2)
                next_layer(p, 1, 1)
                next_aw(p, 3, 3)
                next_layer(p, 3, 2)
                sp.wait_ge(nm_done, 8 * FIRST[1] + 8)
                load_diagonals(p, b0)
                load_residual(p, 6, b0, (0, 1))
                next_aw(p, 5, 0)
                load_residual(p, 6, b0, range(2, NT))
                sp.wait_ge(gd_done, 1)
                load_diagonals(p, b1_)
                sp.wait_ge(x1_done, 8)
                load_residual(p, 7, b1_, (0, 1))
                next_layer(p, 5, 0)
                load_residual(p, 7, b1_, range(2, NT))
                next_aw(p, 7, 1)
                store_out(p, 6, b0)
                sp.wait_ge(out_done, 16 * 8)
                load_graph(0, bn)
                sp.wait_ge(gd_done, 2)
                sp.wait_ge(x1_done, 16)
                sp.wait_ge(xl_done, 8 * 7 + 8)
                load_adj(p, 8, bn)
                store_out(p, 7, b1_)
                sp.wait_ge(out_done, 16 * 16)
                for s, n in ((gb1_ready, 32 + 96), (gb2_ready, 32 + 96), (w_ready, 48),
                             (x0_ready, 16 + 32), (aw_ready[0], 16 + 32), (aw_ready[1], 16 + 32)):
                    sp.wait_ge(s, n)
                sp.wait_ge(arrived, len(go))
                sp.sem_inc(arrived, -len(go))
                for s, n in counts:
                    sp.sem_inc(s, -n)
                for s in go.values():
                    sp.sem_inc(s, 1)

        @block.gpsimd
        def _(pool):
            pool.memset(ident[:, :], 0.0).then_inc(const_ready, 1)
            pool.memset(notib[:, :], 1.0).then_inc(const_ready, 1)
            pool.memset(sel[:, :, :], 0.0).then_inc(const_ready, 1)
            pool.memset(ones3[:, :], 0.0).then_inc(const_ready, 1)
            pool.memset(onesf[:, :], 1.0).then_inc(const_ready, 1)
            pool.memset(mhalf[:, :], -0.5).then_inc(const_ready, 1)
            pool.memset(xh[:, :, :, D:D + 2], 1.0).then_inc(const_ready, 1)
            pool.wait_ge(const_ready, 7)
            pool.affine_select(out=ident[:, :], in_=ident[:, :], compare_op=ALU.not_equal, fill=1.0,
                               base=0, pattern=[[-1, P]], channel_multiplier=1).then_inc(const_ready, 1)
            pool.affine_select(out=notib[:, :], in_=notib[:, :], compare_op=ALU.not_equal, fill=0.0,
                               base=0, pattern=[[-1, P]], channel_multiplier=1).then_inc(const_ready, 1)
            n = 9
            for r in [32 * v + NT * part for v in range(2) for part in range(3)]:
                pool.affine_select(out=sel[:, :, :], in_=sel[:, :, :], compare_op=ALU.not_equal,
                                   fill=1.0, base=-r, pattern=[[-1, NT], [0, P]],
                                   channel_multiplier=1).then_inc(const_ready, 1)
                n += 1
                pool.wait_ge(const_ready, n)
            for r in (0, 32, 64):
                pool.memset(ones3[r:r + 1, :], 1.0).then_inc(const_ready, 1)
            pool.wait_ge(const_ready, 18)
            pool.tensor_copy(identb[:, :], ident[:, :]).then_inc(const_ready, 1)
            pool.wait_ge(const_ready, 19)

            def ln_rstd(p, kind, k, t):
                per, n = ln_at(kind, k, t)
                pool.wait_ge(st_done[kind], at(p, per, n + 1))
                pool.tensor_scalar(ve[:, kind, t:t + 1], mv[:, kind, t, 1:2], 1.0, EPS,
                                   op0=ALU.mult, op1=ALU.add).then_inc(eps_done[kind], 1)
                pool.wait_ge(eps_done[kind], at(p, per, n + 1))
                pool.tensor_tensor(out=rs[:, kind, t:t + 1], in0=ve[:, kind, t:t + 1],
                                   in1=mhalf[:, 0:1], op=ALU.pow).then_inc(pow_done[kind], 1)
                pool.wait_ge(pow_done[kind], at(p, per, n + 1))
                pool.tensor_scalar(nb[:, kind, t:t + 1], mv[:, kind, t, 0:1], rs[:, kind, t:t + 1], -1.0,
                                   op0=ALU.mult, op1=ALU.mult).then_inc(nb_done[kind], 1)

            def affine(p, kind, k, t):
                gb, s = ((gb1, gb1_ready), (gb2, gb2_ready))[kind]
                v = xc[:, k % 2, t, :]
                if t == 0:
                    pool.wait_ge(s, 32 * (k // 2 + 1))
                per, n = ln_at(kind, k, t)
                pool.wait_ge(norm_done[kind], n + 1)
                pool.tensor_tensor(out=v, in0=v, in1=gb[:, 0, :], op=ALU.mult).then_inc(mul_done[kind], 1)
                pool.wait_ge(mul_done[kind], n + 1)
                pool.tensor_tensor(out=v, in0=v, in1=gb[:, 1, :], op=ALU.add).then_inc(aff_done[kind], 1)

            def value(q, t):
                return wv[:, t % 2, :] if layer_of(q) == 3 else xc[:, q % 2, t, :]

            def low(p, q, t):
                pool.wait_ge(xh_done, at(p, 64, 8 * q + t + 1))
                pool.tensor_tensor(out=xl[:, q % 2, t, :], in0=value(q, t), in1=xh[:, q % 2, t, 0:D],
                                   op=ALU.subtract).then_inc(xl_done, 1)

            def mask(p, q, n):
                h, jt = divmod(n, NT)
                if n == 0 and q in FIRST:
                    pool.wait_ge(nmt_done, at(p, 16, 8 * FIRST[q] + 8))
                if n == 0 and layer_of(q) == 3:
                    pool.wait_ge(gdt_done, at(p, 16, 8 * (q - 6) + 8))
                pool.wait_ge(x_done, at(p, 128, 16 * q + n + 1))
                v = xs[:, n % XRING, :]
                pool.tensor_tensor(out=v, in0=v, in1=nmT[:, q % 2, jt, h * HALF:(h + 1) * HALF],
                                   op=ALU.add).then_inc(xm_done, 1)

            def self_edges(p, q, t):
                pool.wait_ge(nm_done, at(p, 16, 8 * FIRST[q] + t + 1))
                d = nm[:, q % 2, t, t * P:(t + 1) * P]
                pool.tensor_tensor(out=d, in0=d, in1=notib[:, :], op=ALU.mult).then_inc(dfix_done, 1)

            def final(p, k, t):
                pool.wait_ge(elu_sum, 8 * (k - 6) + t + 1)
                v = xc[:, k % 2, t, :]
                pool.tensor_tensor(out=v, in0=v, in1=va[:, t % 2, :], op=ALU.add).then_inc(o_ready, 1)

            def first_prep(p, q):
                for t in range(NT):
                    self_edges(p, q, t)
                    ln_rstd(p, LNP, q, t)
                    if t >= 1:
                        low(p, q, t - 1)
                low(p, q, NT - 1)

            def gat_prep_a(p, q, t):
                g = q - 6
                pool.wait_ge(xr_ready[t % 2], 64 * g + 16 * (t // 2 + 1))
                pool.wait_ge(aff_done[1], 8 * (q - 2) + t + 1)
                v = xc[:, q % 2, t, :]
                pool.tensor_tensor(out=v, in0=v, in1=xr[:, t % 2, :], op=ALU.add).then_inc(x1_done, 1)

            def step(p, k):
                q = k + 1
                gat, first = layer_of(q) == 3, q in FIRST
                if gat:
                    gat_prep_a(p, q, 0)
                    gat_prep_a(p, q, 1)
                for t in range(NT):
                    if first or gat:
                        ln_rstd(p, LNP, q, t)
                    if gat and 2 * t + 3 < NT:
                        gat_prep_a(p, q, 2 * t + 2)
                        gat_prep_a(p, q, 2 * t + 3)
                    if k == 7 and t >= 1:
                        final(p, k, t - 1)
                    if k < 6:
                        ln_rstd(p, LN1, k, t)
                        affine(p, LN1, k, t)
                        if 1 <= k <= 4 and t < HT:
                            low(p, k + 1, HT + t)
                    if q == 1:
                        self_edges(p, q, t)
                        if t >= 1:
                            low(p, q, t - 1)
                    if q == 8:
                        if t < HT:
                            self_edges(p, q, 2 * t)
                            self_edges(p, q, 2 * t + 1)
                        if t >= 1:
                            low(p, q, t - 1)
                    if gat:
                        if t % 2 == 1:
                            if t >= 3:
                                low(p, q, t - 3)
                                low(p, q, t - 2)
                    if k == 6 and t >= 1:
                        final(p, k, t - 1)
                if first:
                    low(p, q, NT - 1)
                if gat:
                    low(p, q, NT - 2)
                    low(p, q, NT - 1)
                if k >= 6:
                    final(p, k, NT - 1)
                for h in range(2):
                    for jt in range(AHEAD * h, NT):
                        mask(p, q, NT * h + jt)
                        if k < 6 and jt in (5 - h, 6 - h):
                            ln_rstd(p, LN2, k, HT * h + jt - (5 - h))
                        if k < 6 and h == 1 and jt == 6:
                            affine(p, LN2, k, HT)
                    if k < 6 and h == 0:
                        ln_rstd(p, LN2, k, 2)
                        affine(p, LN2, k, 0)
                        ln_rstd(p, LN2, k, 3)
                        affine(p, LN2, k, 1)
                    elif k < 6:
                        affine(p, LN2, k, HT + 1)
                        for t in (HT + 2, HT + 3):
                            ln_rstd(p, LN2, k, t)
                            affine(p, LN2, k, t)
                    if h == 0:
                        for jt in range(AHEAD):
                            mask(p, q, NT + jt)
                        if k < 6:
                            affine(p, LN2, k, 2)
                            affine(p, LN2, k, 3)
                        if k < 4:
                            for t in range(HT):
                                low(p, k + 2, t)

            first_prep(START, 8)
            for n in range(2 * NT):
                mask(START, 8, n)
            with pool.Fori(0, PAIRS) as p:
                for k in range(8):
                    step(p, k)
                pair_end(pool, "pool")

        @block.scalar
        def _(act):
            def normalise(p, kind, k, t):
                per, n = ln_at(kind, k, t)
                act.wait_ge(nb_done[kind], at(p, per, n + 1))
                src = xc[:, k % 2, t, :]
                dst = src
                if kind == LNP and layer_of(k) == 3:
                    dst = xg[:, t % 2, :]
                    if t == 0:
                        act.wait_ge(f2_done, at(p, 48, 8 * (k - 1)))
                    if t >= 2:
                        act.wait_ge(pt_done, at(p, 8, 4 * (k - 6) + t // 2))
                act.activation(dst, src, ACT.Relu if kind == LNP else ACT.Identity,
                               bias=nb[:, kind, t:t + 1], scale=rs[:, kind, t:t + 1])\
                   .then_inc(norm_done[kind], 1)

            def high(p, q, t):
                if q in FIRST:
                    per, n = ln_at(LNP, q, t)
                    act.wait_ge(norm_done[LNP], at(p, per, n + 1))
                    src = xc[:, q % 2, t, :]
                elif layer_of(q) == 3:
                    act.wait_ge(wv_done, at(p, 8, 4 * (q - 6) + t // 2 + 1))
                    src = wv[:, t % 2, :]
                else:
                    act.wait_ge(aff_done[1], at(p, 48, 8 * (q - 2) + t + 1))
                    src = xc[:, q % 2, t, :]
                act.activation(xh[:, q % 2, t, 0:D], src, ACT.Copy).then_inc(xh_done, 1)

            def ht_high(p, k, j):
                act.wait_ge(ht_done, 4 * k + j + 1)
                act.activation(hTh[:, :, 2 * P * (j % 2):2 * P * (j % 2 + 1)], TH[:, :, :], ACT.Copy)\
                   .then_inc(hth_done, 1)

            def gelu(p, k, h, f):
                n = 16 * k + FT * h + f
                act.wait_ge(f1_done, n + 1)
                if not (h == 0 and f < 2):
                    act.wait_ge(glo_done, n - 1)
                act.activation(g32[:, f % 2, :], FB[f % 2][:, :], ACT.Gelu, bias=b1c[:, k // 2, f:f + 1],
                               scale=1.0 / W_SCALE).then_inc(gelu_done, 1)
                act.wait_ge(gelu_done, n + 1)
                act.activation(gT[:, 0, f, :], g32[:, f % 2, :], ACT.Copy).then_inc(ghi_done, 1)

            def exps(p, q, h, k=None):
                def phi(n):
                    jt = n % NT
                    act.wait_ge(exp_done, at(p, 128, 16 * q + n + 1))
                    act.activation(pH[:, jt, h * HALF:(h + 1) * HALF], xs[:, n % XRING, :], ACT.Copy)\
                       .then_inc(phi_done, 1)

                if p is START:
                    act.wait_ge(w_split, 2 * LAYERS)
                else:
                    act.wait_ge(agg_done, 8 * (q - 1) + HT * h + HT)
                for jt in range(NT):
                    n = NT * h + jt
                    act.wait_ge(xm_done, at(p, 128, 16 * q + n + 1))
                    v = xs[:, n % XRING, :]
                    act.activation(v, v, ACT.Exp, bias=sj2[:, jt:jt + 1]).then_inc(exp_done, 1)
                    phi(n)
                    if k is not None and h == 0 and jt == 3:
                        ht_high(p, k, 3)
                    if k is not None and jt in (6 - h, 7 - h):
                        normalise(p, LN2, k, HT * h + jt - (6 - h))

            def r2_copy(p, q):
                act.wait_ge(row_done, at(p, 24, 3 * q + 2))
                act.activation(r2s[:, :], RB[:, :], ACT.Copy).then_inc(r2_done, 1)

            def mask_copy(p, q, jt):
                act.wait_ge(mt_done, at(p, 16, 8 * FIRST[q] + jt + 1))
                act.activation(nmT[:, q % 2, jt, :], TPb[:, :], ACT.Copy).then_inc(nmt_done, 1)

            def gat_diag_copy(p, q):
                act.wait_ge(gt_done, q - 6 + 1)
                for t in range(NT):
                    act.activation(nmT[:, q % 2, t, t * P:(t + 1) * P], TPb[:, t * P:(t + 1) * P],
                                   ACT.Copy).then_inc(gdt_done, 1)

            def gat_pair(p, q, j):
                g = q - 6
                act.wait_ge(pt_done, 4 * g + j + 1)
                act.activation(xgT[:, 0, :, :], TP[:, :, :], ACT.Copy).then_inc(pth_done, 1)

            def gat_values(p, q, j):
                g = q - 6
                act.wait_ge(wh_done, 4 * g + j + 1)
                if j >= 1:
                    act.wait_ge(xl_done, 8 * q + 2 * j)
                    act.wait_ge(sc_done, 8 * q + 2 * j)
                act.activation(wv[:, :, :].rearrange("p a d -> p (a d)"), TPf[:, :], ACT.Copy,
                               scale=1.0 / W_SCALE)\
                   .then_inc(wv_done, 1)
                high(p, q, 2 * j)
                high(p, q, 2 * j + 1)

            def elu(p, k, t):
                act.wait_ge(elu_min, 8 * (k - 6) + t + 1)
                act.activation(vn[:, t % 2, :], vn[:, t % 2, :], ACT.Exp).then_inc(elu_exp, 1)

            def step(p, k):
                q = k + 1
                gat, first = layer_of(q) == 3, q in FIRST
                if gat:
                    gat_diag_copy(p, q)
                for t in range(NT):
                    if k < 6 and t in (4, 6):
                        ht_high(p, k, t // 2 - 2)
                    if q == 8 and t >= HT:
                        mask_copy(p, q, 2 * (t - HT))
                    if first or gat:
                        normalise(p, LNP, q, t)
                    if first:
                        high(p, q, t)
                    if k < 6:
                        normalise(p, LN1, k, t)
                        if 1 <= k <= 4 and t < 2:
                            high(p, k + 1, NT - 2 + t)
                    if k == 7:
                        if t >= HT:
                            mask_copy(p, q, 2 * (t - HT) + 1)
                        elu(p, k, t)
                    if gat:
                        if t % 2 == 1:
                            if t >= 3:
                                gat_values(p, q, t // 2 - 1)
                            gat_pair(p, q, t // 2)
                    if k == 6:
                        elu(p, k, t)
                if gat:
                    gat_values(p, q, NT // 2 - 1)
                if k < 6:
                    for f in range(FT):
                        gelu(p, k, 0, f)
                        if first:
                            mask_copy(p, q, f)
                        if q not in RAW and f == 3:
                            r2_copy(p, q)
                if q in RAW:
                    r2_copy(p, q)
                if k < 6:
                    ht_high(p, k, 2)
                for h in range(2):
                    exps(p, q, h, k if k < 6 else None)
                    if k < 6 and h == 0:
                        for f in range(FT):
                            gelu(p, k, 1, f)
                            if f < 2:
                                normalise(p, LN2, k, 2 + f)
                            if k < 4 and f % 2 == 1:
                                high(p, k + 2, f // 2)
                    elif k < 6:
                        for t in (HT + 2, HT + 3):
                            normalise(p, LN2, k, t)
                            if k < 4:
                                high(p, k + 2, t - 2)

            act.wait_ge(const_ready, 19)
            for t in range(NT):
                normalise(START, LNP, 8, t)
                high(START, 8, t)
            for jt in range(NT):
                mask_copy(START, 8, jt)
            r2_copy(START, 8)
            exps(START, 8, 0)
            exps(START, 8, 1)
            with act.Fori(0, PAIRS) as p:
                for k in range(8):
                    step(p, k)
                pair_end(act, "act")

        @block.vector
        def _(dve):
            COLS = 13

            def statistics(p, kind, k, t):
                per, n = ln_at(kind, k, t)
                dve.bn_stats(st[:, kind, t, :], xc[:, k % 2, t, :]).then_inc(bs_done[kind], 1)
                dve.wait_ge(bs_done[kind], at(p, per, n + 1))
                dve.bn_aggr(mv[:, kind, t, :], st[:, kind, t, :]).then_inc(st_done[kind], 1)

            def residual1(p, k, t):
                dve.wait_ge(agg_done, 8 * k + t + 1)
                o = OB[t % 2]
                dve.reciprocal(rden[:, t:t + 1], o[:, D:D + 1]).then_inc(rden_done, 1)
                dve.wait_ge(rden_done, 8 * k + t + 1)
                v = xc[:, k % 2, t, :]
                dve.scalar_tensor_tensor(out=v, in0=o[:, 0:D], scalar=rden[:, t:t + 1], in1=v,
                                         op0=ALU.mult, op1=ALU.add).then_inc(ob_free, 1)
                dve.wait_ge(ob_free, CREDIT + user(k) + t + 1)
                statistics(p, LN1, k, t)

            def residual2(p, k, t):
                dve.wait_ge(f2_done, 8 * k + t + 1)
                dve.wait_ge(aff_done[0], 8 * k + t + 1)
                v = xc[:, k % 2, t, :]
                dve.scalar_tensor_tensor(out=v, in0=OB[t % 2][:, 0:D], scalar=1.0 / W_SCALE, in1=v,
                                         op0=ALU.mult, op1=ALU.add).then_inc(ob_free, 1)

            def statistics2(p, k, t):
                dve.wait_ge(ob_free, CREDIT + user(k) + NT + t + 1)
                statistics(p, LN2, k, t)

            def scores(p, q, t):
                l = layer_of(q)
                if q in FIRST:
                    per, n = ln_at(LNP, q, t)
                    dve.wait_ge(norm_done[LNP], at(p, per, n + 1))
                    src = xc[:, q % 2, t, :]
                elif l == 3:
                    dve.wait_ge(wv_done, at(p, 8, 4 * (q - 6) + t // 2 + 1))
                    src = wv[:, t % 2, :]
                else:
                    dve.wait_ge(aff_done[1], at(p, 48, 8 * (q - 2) + t + 1))
                    src = xc[:, q % 2, t, :]
                if t == 0:
                    dve.wait_ge(aw_ready[l % 2], at(p, 32, 16 * (1 + ((q + 2) // 4 if l % 2 == 0 else q // 6))))
                dve.wait_ge(si_done, at(p, 64, 8 * q + t))
                dve.tensor_tensor_reduce(out=junk[:, 0, :], in0=src, in1=aw[:, l % 2, 0, :], scale=1.0,
                                         scalar=0.0, op0=ALU.mult, op1=ALU.add,
                                         accum_out=sc[:, q % 2, 0, t:t + 1]).then_inc(si_done, 1)
                dve.wait_ge(sc_done, at(p, 64, 8 * q + t))
                dve.tensor_tensor_reduce(out=junk[:, 1, :], in0=src, in1=aw[:, l % 2, 1, :], scale=1.0,
                                         scalar=0.0, op0=ALU.mult, op1=ALU.add,
                                         accum_out=sc[:, q % 2, 1, t:t + 1]).then_inc(sc_done, 1)

            def col(p, q, i, ins):
                ins.then_inc(col_step, 1)
                dve.wait_ge(col_step, at(p, 8 * COLS, COLS * q + i))

            def split3(p, q, i, src, nv):
                col(p, q, i, dve.tensor_copy(c3[:, 0:nv, 0, :], src))
                col(p, q, i + 1, dve.tensor_tensor(out=cr[:, 0:nv, :], in0=src, in1=c3[:, 0:nv, 0, :],
                                                   op=ALU.subtract))
                col(p, q, i + 2, dve.tensor_copy(c3[:, 0:nv, 1, :], cr[:, 0:nv, :]))
                dve.tensor_tensor(out=c3[:, 0:nv, 2, :], in0=cr[:, 0:nv, :], in1=c3[:, 0:nv, 1, :],
                                  op=ALU.subtract).then_inc(c3_done, 1)

            def sj_columns(p, q):
                dve.wait_ge(sc_done, at(p, 64, 8 * q + 8))
                sj = sc[:, q % 2, 1, :]
                split3(p, q, 1, sc[:, q % 2, 1:2, :], 1)
                col(p, q, 4, dve.tensor_scalar(sj8[:, :], sj, 1.0 - SLOPE, None, ALU.mult))
                col(p, q, 5, dve.tensor_scalar(sj2[:, :], sj, SLOPE, P_LOG, ALU.mult, ALU.add))

            def cT_copy(p, q, i):
                dve.wait_ge(ct_done, at(p, 16, 2 * q + i))
                dve.tensor_copy(cT[:, :], TPb[0:64, 0:P]).then_inc(cT_done, 1)

            def row_max(p, q, t):
                if t == 0:
                    dve.wait_ge(row_done, at(p, 24, 3 * q + 1))
                    dve.wait_ge(plo_done, at(p, 128, 16 * q))
                    if q in FIRST:
                        dve.wait_ge(dfix_done, at(p, 16, 8 * FIRST[q] + 8))
                if t >= XRING:
                    dve.wait_ge(max_done, at(p, 64, 8 * q + t - XRING + 1))
                dve.tensor_tensor_reduce(out=xs[:, t % XRING, :].bitcast(bf16), in0=RB[:, :],
                                         in1=nm[:, q % 2, t, :], scale=1.0, scalar=-3e38, op0=ALU.add,
                                         op1=ALU.max, accum_out=M[:, t:t + 1]).then_inc(max_done, 1)

            def r_columns(p, q):
                dve.wait_ge(max_done, at(p, 64, 8 * q + 8))
                si = sc[:, q % 2, 0, :]
                l = layer_of(q)
                if l == 3:
                    g = q - 6
                    dve.tensor_scalar(ef[:, q % 2, :], M[:, :], NOEDGE / 2, None, ALU.is_lt)\
                       .then_inc(gcol_step, 1)
                    dve.tensor_scalar(ne[:, :], M[:, :], NOEDGE / 2, None, ALU.is_ge)\
                       .then_inc(gcol_step, 1)
                    dve.wait_ge(gcol_step, 3 * g + 2)
                    dve.tensor_tensor(out=M[:, :], in0=M[:, :], in1=ne[:, :], op=ALU.mult)\
                       .then_inc(gcol_step, 1)
                    dve.wait_ge(gcol_step, 3 * g + 3)
                    col(p, q, 6, dve.tensor_copy(s1[:, :], si))
                else:
                    col(p, q, 6, dve.tensor_scalar(s1[:, :], si, ab[:, l:l + 1], None, ALU.add))
                col(p, q, 7, dve.tensor_tensor(out=um[:, 0, :], in0=s1[:, :], in1=M[:, :], op=ALU.add))
                col(p, q, 8, dve.scalar_tensor_tensor(out=um[:, 1, :], in0=um[:, 0, :], scalar=SLOPE,
                                                      in1=um[:, 0, :], op0=ALU.mult, op1=ALU.max))
                col(p, q, 9, dve.tensor_tensor(out=R[:, 0, :], in0=s1[:, :], in1=um[:, 1, :],
                                               op=ALU.subtract))
                col(p, q, 10, dve.scalar_tensor_tensor(out=R[:, 1, :], in0=s1[:, :], scalar=SLOPE,
                                                       in1=um[:, 1, :], op0=ALU.mult, op1=ALU.subtract))
                dve.wait_ge(ct_done, at(p, 16, 2 * q + 1))
                split3(p, q, 11, R[:, :, :], 2)

            def score(p, q, n):
                h, jt = divmod(n, NT)
                if n == 0:
                    dve.wait_ge(row_done, at(p, 24, 3 * q + 3))
                    dve.wait_ge(r2_done, at(p, 8, q + 1))
                if n >= XRING:
                    dve.wait_ge(plo_done, at(p, 128, 16 * q + n - XRING + 1))
                half = slice(h * HALF, (h + 1) * HALF)
                dve.scalar_tensor_tensor(out=xs[:, n % XRING, :], in0=RB[:, half], scalar=sj8[:, jt:jt + 1],
                                         in1=r2s[:, half], op0=ALU.add, op1=ALU.max)\
                   .then_inc(x_done, 1)

            def p_low(p, q, n):
                h, jt = divmod(n, NT)
                half = slice(h * HALF, (h + 1) * HALF)
                dve.wait_ge(phi_done, at(p, 128, 16 * q + n + 1))
                dve.tensor_tensor(out=pL[:, jt, half], in0=xs[:, n % XRING, :], in1=pH[:, jt, half],
                                  op=ALU.subtract).then_inc(plo_done, 1)

            def weights(p, q, i, h):
                lag = XRING - 1
                if AHEAD <= i < NT:
                    score(p, q, NT * h + i)
                if i >= lag:
                    p_low(p, q, NT * h + i - lag)
            SLOTS = NT + XRING - 1
            RESIDUALS = ((4, 5, 7, 9), (3, 4, 6, 8))
            ROW_MAX = ((), (), (), (0,), (1,), (2, 3), (4, 5), (6, 7))
            RAW_MAX = ((), (), (0,), (1,), (2, 3), (4,), (5, 6), (7,))

            def ht_low(p, k, j):
                dve.wait_ge(hth_done, 4 * k + j + 1)
                cols = slice(2 * P * (j % 2), 2 * P * (j % 2 + 1))
                dve.tensor_tensor(out=hTl[:, :, cols], in0=TH[:, :, :], in1=hTh[:, :, cols],
                                  op=ALU.subtract).then_inc(htl_done, 1)

            def g_low(p, k, h, f):
                dve.wait_ge(ghi_done, 16 * k + FT * h + f + 1)
                dve.tensor_tensor(out=gT[:, 1, f, :], in0=g32[:, f % 2, :], in1=gT[:, 0, f, :],
                                  op=ALU.subtract).then_inc(glo_done, 1)

            def edges(p, q, t):
                a = FIRST[q]
                dve.wait_ge(adj_ready[t % 2], at(p, 128, 64 * a + 16 * (t // 2 + 1)))
                dve.tensor_scalar(nm[:, q % 2, t, :], adjst[:, t % 2, :], 0.0, NOEDGE, ALU.is_equal,
                                  ALU.mult).then_inc(nm_done, 1)

            def raw_statistics(p, q, t):
                a = FIRST[q]
                if t == 0:
                    dve.wait_ge(x0_ready, at(p, 32, 16 * (a + 1)))
                statistics(p, LNP, q, t)

            def gat_edges(p, q):
                g = q - 6
                dve.wait_ge(diag_ready, 128 * (g + 1))
                for t in range(NT):
                    ins = dve.tensor_scalar(nm[:, q % 2, t, t * P:(t + 1) * P], adjd[:, t, :], 0.0,
                                            NOEDGE, ALU.is_equal, ALU.mult)
                ins.then_inc(gd_done, 1)

            def gat_statistics(p, q, t):
                dve.wait_ge(x1_done, 8 * (q - 6) + t + 1)
                statistics(p, LNP, q, t)

            def gat_low(p, q, j):
                g = q - 6
                dve.wait_ge(pth_done, 4 * g + j + 1)
                dve.tensor_tensor(out=xgT[:, 1, :, :], in0=TP[:, :, :], in1=xgT[:, 0, :, :],
                                  op=ALU.subtract).then_inc(ptl_done, 1)

            def gat_sum(p, q):
                dve.wait_ge(cs_done, q - 6 + 1)
                dve.tensor_copy(csum[:, q % 2, :], TPf[:, 0:D]).then_inc(csc_done, 1)

            def elu_a(p, k, t):
                n = 8 * (k - 6) + t + 1
                s = k % 2
                dve.wait_ge(agg_done, 8 * k + t + 1)
                if t == 0:
                    dve.wait_ge(csc_done, k - 6 + 1)
                o = OB[t % 2]
                if n > 2:
                    dve.wait_ge(o_ready, n - 2)
                e = ef[:, s, t:t + 1]
                dve.scalar_tensor_tensor(out=den[:, t:t + 1], in0=e, scalar=float(N), in1=o[:, D:D + 1],
                                         op0=ALU.mult, op1=ALU.add).then_inc(den_done, 1)
                dve.scalar_tensor_tensor(out=v2[:, t % 2, :], in0=csum[:, s, :], scalar=e,
                                         in1=o[:, 0:D], op0=ALU.mult, op1=ALU.add)\
                   .then_inc(ob_free, 1)
                dve.wait_ge(den_done, n)
                dve.reciprocal(rden[:, t:t + 1], den[:, t:t + 1]).then_inc(rden_done_g, 1)
                dve.wait_ge(rden_done_g, n)
                dve.wait_ge(ob_free, CREDIT + user(k) + t + 1)
                dve.tensor_scalar(vn[:, t % 2, :], v2[:, t % 2, :], rden[:, t:t + 1], 0.0, ALU.mult,
                                  ALU.min).then_inc(elu_min, 1)
                dve.tensor_scalar(va[:, t % 2, :], v2[:, t % 2, :], rden[:, t:t + 1], 0.0, ALU.mult,
                                  ALU.max).then_inc(elu_max, 1)

            def elu_b(p, k, t):
                n = 8 * (k - 6) + t + 1
                dve.wait_ge(elu_exp, n)
                dve.wait_ge(elu_max, n)
                dve.scalar_tensor_tensor(out=va[:, t % 2, :], in0=vn[:, t % 2, :], scalar=-1.0,
                                         in1=va[:, t % 2, :], op0=ALU.add, op1=ALU.add)\
                   .then_inc(elu_sum, 1)

            def step(p, k):
                q = k + 1
                gat, first = layer_of(q) == 3, q in FIRST
                if gat:
                    gat_edges(p, q)
                    gat_statistics(p, q, 0)
                    gat_statistics(p, q, 1)
                for t in range(NT):
                    if q == 8 or (q == 1 and t >= 1):
                        raw_statistics(p, q, t)
                    if k < 6:
                        residual1(p, k, t)
                    else:
                        elu_a(p, k, t)
                        if t >= 1:
                            elu_b(p, k, t - 1)
                    if k < 6 and t in (4, 6):
                        ht_low(p, k, t // 2 - 2)
                    if q not in RAW:
                        if t < 2:
                            scores(p, q, NT - 2 + t)
                        if t == 1:
                            sj_columns(p, q)
                        if t == 2:
                            cT_copy(p, q, 1)
                        for i in ROW_MAX[t]:
                            row_max(p, q, i)
                    if q == 1:
                        if t == 0:
                            raw_statistics(p, q, t)
                        edges(p, q, t)
                    if q == 8:
                        if t < HT:
                            edges(p, q, 2 * t)
                            edges(p, q, 2 * t + 1)
                    if first and t >= 1:
                        scores(p, q, t - 1)
                    if gat and 2 * t + 3 < NT:
                        gat_statistics(p, q, 2 * t + 2)
                        gat_statistics(p, q, 2 * t + 3)
                    if gat and t % 2 == 1:
                        gat_low(p, q, t // 2)
                        if t >= 3:
                            scores(p, q, t - 3)
                            scores(p, q, t - 2)
                if k >= 6:
                    elu_b(p, k, NT - 1)
                if gat:
                    scores(p, q, NT - 2)
                if q in RAW:
                    scores(p, q, NT - 1)
                    sj_columns(p, q)
                    if first:
                        cT_copy(p, q, 1)
                if q not in RAW:
                    r_columns(p, q)
                if k < 6:
                    for f in range(FT):
                        g_low(p, k, 0, f)
                        if q not in RAW and f == 2:
                            cT_copy(p, q, 2)
                        if q not in RAW and f >= FT - AHEAD:
                            score(p, q, f - (FT - AHEAD))
                        if gat and f == 1:
                            gat_sum(p, q)
                            cT_copy(p, q, 1)
                        if q in RAW and f >= 2:
                            for i in RAW_MAX[f]:
                                row_max(p, q, i)
                if q in RAW:
                    if k >= 6 and gat:
                        gat_sum(p, q)
                        cT_copy(p, q, 1)
                    if k >= 6:
                        for t in range(NT):
                            row_max(p, q, t)
                    r_columns(p, q)
                    cT_copy(p, q, 2)
                    for n in range(AHEAD):
                        score(p, q, n)
                if k < 6:
                    ht_low(p, k, 2)
                for h in range(2):
                    for i in range(SLOTS):
                        weights(p, q, i, h)
                        if k < 6 and h == 0 and i == 5:
                            ht_low(p, k, 3)
                        if k < 6 and i in RESIDUALS[h]:
                            t = HT * h + RESIDUALS[h].index(i)
                            residual2(p, k, t)
                            statistics2(p, k, t)
                    if h == 0:
                        for n in range(AHEAD):
                            score(p, q, NT + n)
                    if k < 6 and h == 0:
                        for t in range(HT):
                            g_low(p, k, 1, 2 * t)
                            g_low(p, k, 1, 2 * t + 1)
                            if k < 4:
                                scores(p, k + 2, t)
                    elif k < 4:
                        for t in (HT, HT + 1):
                            scores(p, k + 2, t)

            dve.memset(c3[:, :, :, :], 0.0).then_inc(w_zero, 1)
            dve.memset(b2r[:, :, :], 0.0).then_inc(w_zero, 1)
            dve.wait_ge(w_zero, 2)
            dve.wait_ge(const_ready, 19)
            for _ in range(CREDIT):
                dve.sem_inc(ob_free, 1)
            for t in range(NT):
                edges(START, 8, t)
                raw_statistics(START, 8, t)
            dve.wait_ge(raw_ready, 16 * (1 + 1 + 1 + 1 + 6))
            for t in range(NT):
                scores(START, 8, t)
            sj_columns(START, 8)
            b2f, b2p = r2s[:, 0:LAYERS * D], xs[:, 0:2, :].rearrange("p a b -> p (a b)")[:, 0:LAYERS * D]
            b2b = xs[:, 2, :].bitcast(bf16)[:, 0:LAYERS * D]
            b2c = b2r[:, :, :].rearrange("p l d -> p (l d)")

            def link(n, ins):
                ins.then_inc(b2_step, 1)
                dve.wait_ge(b2_step, n)

            link(1, dve.tensor_scalar(b2p, b2f, W_SCALE, None, ALU.mult))
            for part in range(3):
                link(3 * part + 2, dve.tensor_copy(b2b, b2p))
                link(3 * part + 3, dve.tensor_tensor(out=b2p, in0=b2p, in1=b2b, op=ALU.subtract))
                r = 32 * part
                link(3 * part + 4, dve.tensor_copy(b2c[r:r + 1, :], b2b[r:r + 1, :]))
            dve.wait_ge(b1t_done, 1)
            dve.tensor_copy(b1c[:, :, :].rearrange("p l f -> p (l f)"), TH[:, 0, 0:LAYERS * FT])
            gwf = g32[:, 0, :]
            gwh, gwl = (gw[:, i, :, :].rearrange("p k d -> p (k d)") for i in range(2))
            link(11, dve.tensor_scalar(gwh, gwf, W_SCALE, None, ALU.mult))
            link(12, dve.scalar_tensor_tensor(out=gwl, in0=gwf, scalar=W_SCALE, in1=gwh, op0=ALU.mult,
                                              op1=ALU.subtract))
            raws = [pL[:, :, :].bitcast(f32).rearrange("p a b -> p (a b)"),
                    pH[:, :, :].bitcast(f32).rearrange("p a b -> p (a b)"),
                    nmT[:, 1, :, :].bitcast(f32).rearrange("p a b -> p (a b)")]
            splits = [wb[:, :, :], gT[:, :, :, :].rearrange("p a f n -> p (a f n)").rearrange(
                          "p (a b) -> p a b", a=4),
                      nm[:, 1, :, :].rearrange("p t n -> p (t n)").bitcast(f16).rearrange(
                          "p (a b) -> p a b", a=4)]
            for l in range(LAYERS):
                w = splits[l].rearrange("p (m i) b -> p m i b", i=2)
                raw = raws[l].rearrange("p (m b) -> p m b", m=2)
                dve.tensor_scalar(w[:, :, 0, :], raw, W_SCALE, None, ALU.mult).then_inc(w_split, 1)
                dve.wait_ge(w_split, 2 * l + 1)
                dve.scalar_tensor_tensor(out=w[:, :, 1, :], in0=raw, scalar=W_SCALE, in1=w[:, :, 0, :],
                                         op0=ALU.mult, op1=ALU.subtract).then_inc(w_split, 1)
            dve.wait_ge(w_split, 2 * LAYERS)
            dve.wait_ge(w_stored, 16 * LAYERS)
            cT_copy(START, 8, 1)
            for t in range(NT):
                row_max(START, 8, t)
            r_columns(START, 8)
            cT_copy(START, 8, 2)
            for h in range(2):
                for n in range(AHEAD):
                    score(START, 8, NT * h + n)
                for i in range(SLOTS):
                    weights(START, 8, i, h)
            with dve.Fori(0, PAIRS) as p:
                for k in range(8):
                    step(p, k)
                pair_end(dve, "dve")

        @block.tensor
        def _(pe):
            def mm(o, lhsT, rhs, first, last):
                return pe.matmul(o, lhsT, rhs, start=first, stop=last)

            def aggregate(p, k, t):
                s, h = k % 2, t // HT
                if t == 0:
                    pe.wait_ge(xl_done, 8 * k + 8)
                if t % HT == 0:
                    pe.wait_ge(plo_done, 16 * k + NT * (h + 1))
                pe.wait_ge(ob_free, user(k) + t + 1)
                o = OB[t % 2]
                rows = slice(t * P, (t + 1) * P)
                for jt in range(NT):
                    mm(o[:, 0:D + 1], pH[:, jt, rows], xh[:, s, jt, 0:D + 1], jt == 0, False)
                    mm(o[:, 0:D], pH[:, jt, rows], xl[:, s, jt, :], False, False)
                    ins = mm(o[:, 0:D + 1], pL[:, jt, rows], xh[:, s, jt, 0:D + 1], False, jt == NT - 1)
                ins.then_inc(agg_done, 1)

            def transpose_h(p, k, j):
                pe.wait_ge(aff_done[0], 8 * k + 2 * j + 2)
                if j >= 1:
                    pe.wait_ge(htl_done, 4 * k + j)
                for i in range(2):
                    for d in range(KD):
                        ins = pe.transpose(TH[:, d, i * P:(i + 1) * P],
                                           xc[:, k % 2, 2 * j + i, d * P:(d + 1) * P], ident[:, :])
                ins.then_inc(ht_done, 1)

            def hidden(p, k, h, f):
                n = FT * h + f
                if n == 0 and k % 2 == 0 and k > 0:
                    pe.wait_ge(w_ready, 16 * (k // 2))
                if f == 0:
                    pe.wait_ge(htl_done, 4 * k + 2 * h + 2)
                if not (h == 0 and f < 2):
                    pe.wait_ge(gelu_done, 16 * k + n - 1)
                o = FB[f % 2]
                for kd in range(KD):
                    wh = wb[:, 0, kd * FF + f * P:kd * FF + (f + 1) * P]
                    wl = wb[:, 1, kd * FF + f * P:kd * FF + (f + 1) * P]
                    mm(o[:, :], wh, hTh[:, kd, :], kd == 0, False)
                    mm(o[:, :], wh, hTl[:, kd, :], False, False)
                    ins = mm(o[:, :], wl, hTh[:, kd, :], False, kd == KD - 1)
                ins.then_inc(f1_done, 1)

            def second(p, k, t, fs):
                h = t // HT
                o = OB[t % 2][:, 0:D]
                if fs[0] == 0:
                    pe.wait_ge(ob_free, user(k) + NT + t + 1)
                    mm(o, ones3[:, :], b2r[:, k // 2, :], True, False)
                rows = slice((t % HT) * P, (t % HT + 1) * P)
                for f in fs:
                    if t % HT == 0:
                        pe.wait_ge(glo_done, 16 * k + FT * h + f + 1)
                    w2h, w2l = wb[:, 2, f * D:(f + 1) * D], wb[:, 3, f * D:(f + 1) * D]
                    mm(o, gT[:, 0, f, rows], w2h, False, False)
                    mm(o, gT[:, 0, f, rows], w2l, False, False)
                    ins = mm(o, gT[:, 1, f, rows], w2h, False, f == FT - 1)
                if fs[-1] == FT - 1:
                    ins.then_inc(f2_done, 1)

            def second_half(p, k, h, q=None):
                if h == 0:
                    transpose_h(p, k, 2)
                for fs in (range(0, 4), range(4, 6), range(6, 7), range(7, 8)):
                    second(p, k, HT * h, fs)
                    second(p, k, HT * h + 1, fs)
                if q is not None:
                    transpose_c(p, q, 2)
                    spread_r2(p, q)
                    spread_r1(p, q)
                if h == 0:
                    transpose_h(p, k, 3)
                second(p, k, HT * h + 2, range(FT))
                second(p, k, HT * h + 3, range(FT))

            def transpose_c(p, q, i):
                pe.wait_ge(c3_done, at(p, 16, 2 * q + i))
                if (i, q) in ((2, 1), (1, 8)):
                    pe.wait_ge(nmt_done, at(p, 16, 8 * FIRST[q] + 8))
                if i == 1 and layer_of(q) == 3:
                    pe.wait_ge(csc_done, at(p, 2, q - 6 + 1))
                pe.transpose(TPb[0:64, 0:P], c3[:, :, :, :].rearrange("p v a t -> p (v a t)"),
                             identb[:, :]).then_inc(ct_done, 1)

            def spread(p, q, v, i):
                for t in range(NT):
                    ins = mm(RB[:, t * P:(t + 1) * P], sel[32 * v:32 * v + 32, t, :],
                             cT[32 * v:32 * v + 32, :], True, True)
                ins.then_inc(row_done, 1)

            def spread_sj(p, q):
                pe.wait_ge(cT_done, at(p, 16, 2 * q + 1))
                pe.wait_ge(x_done, at(p, 128, 16 * q))
                spread(p, q, 0, 1)

            def spread_r2(p, q):
                pe.wait_ge(cT_done, at(p, 16, 2 * q + 2))
                spread(p, q, 1, 2)

            def spread_r1(p, q):
                pe.wait_ge(r2_done, at(p, 8, q + 1))
                spread(p, q, 0, 3)

            def transpose_mask(p, q, jt):
                a = FIRST[q]
                if jt == 0:
                    pe.wait_ge(dfix_done, at(p, 16, 8 * a + 8))
                    if p is not START:
                        pe.wait_ge(cT_done, 2 * q + 1 if q == 1 else 2 * q)
                else:
                    pe.wait_ge(nmt_done, at(p, 16, 8 * a + jt))
                for it in range(NT):
                    ins = pe.transpose(TPb[:, it * P:(it + 1) * P],
                                       nm[:, q % 2, it, jt * P:(jt + 1) * P], identb[:, :])
                ins.then_inc(mt_done, 1)

            def transpose_diag(p, q):
                pe.wait_ge(gd_done, q - 6 + 1)
                for t in range(NT):
                    ins = pe.transpose(TPb[:, t * P:(t + 1) * P],
                                       nm[:, q % 2, t, t * P:(t + 1) * P], identb[:, :])
                ins.then_inc(gt_done, 1)

            def gat_transpose(p, q, j):
                g = q - 6
                pe.wait_ge(norm_done[LNP], 8 * RAW[q] + 2 * j + 2)
                if j == 0:
                    pe.wait_ge(gdt_done, 8 * g + 8)
                else:
                    pe.wait_ge(wv_done, 4 * g + j)
                for i in range(2):
                    for d in range(KD):
                        ins = pe.transpose(TP[:, d, i * P:(i + 1) * P], xg[:, i, d * P:(d + 1) * P],
                                           ident[:, :])
                ins.then_inc(pt_done, 1)

            def gat_product(p, q, j):
                g = q - 6
                pe.wait_ge(ptl_done, 4 * g + j + 1)
                for i in range(2):
                    o = TPf[:, i * D:(i + 1) * D]
                    rows = slice(i * P, (i + 1) * P)
                    for kd in range(KD):
                        mm(o, xgT[:, 0, kd, rows], gw[:, 0, kd, :], kd == 0, False)
                        mm(o, xgT[:, 0, kd, rows], gw[:, 1, kd, :], False, False)
                        ins = mm(o, xgT[:, 1, kd, rows], gw[:, 0, kd, :], False, kd == KD - 1)
                ins.then_inc(wh_done, 1)

            def gat_colsum(p, q):
                pe.wait_ge(xl_done, 8 * q + 8)
                for jt in range(NT):
                    mm(TPf[:, 0:D], onesf[:, :], xh[:, q % 2, jt, 0:D], jt == 0, False)
                    ins = mm(TPf[:, 0:D], onesf[:, :], xl[:, q % 2, jt, :], False, jt == NT - 1)
                ins.then_inc(cs_done, 1)

            def step(p, k):
                q = k + 1
                gat, first = layer_of(q) == 3, q in FIRST
                if gat:
                    transpose_diag(p, q)
                for t in range(NT):
                    if q == 8 and t >= HT:
                        transpose_mask(p, q, 2 * (t - HT))
                    aggregate(p, k, t)
                    if k < 6 and t in (4, 6):
                        transpose_h(p, k, t // 2 - 2)
                    if q not in RAW and t == 2:
                        transpose_c(p, q, 1)
                        spread_sj(p, q)
                    if gat:
                        if t % 2 == 1:
                            gat_transpose(p, q, t // 2)
                        elif t >= 2:
                            gat_product(p, q, t // 2 - 1)
                    if q == 8 and t >= HT:
                        transpose_mask(p, q, 2 * (t - HT) + 1)
                if gat:
                    gat_product(p, q, NT // 2 - 1)
                if first:
                    transpose_c(p, q, 1)
                    spread_sj(p, q)
                if k < 6:
                    for f in range(FT):
                        hidden(p, k, 0, f)
                        if first:
                            transpose_mask(p, q, f)
                        if q not in RAW:
                            if f == 2:
                                transpose_c(p, q, 2)
                            if f == 3:
                                spread_r2(p, q)
                            if f == 5:
                                spread_r1(p, q)
                        if gat and f == 1:
                            gat_colsum(p, q)
                            transpose_c(p, q, 1)
                            spread_sj(p, q)
                elif gat:
                    gat_colsum(p, q)
                if gat and k >= 6:
                    transpose_c(p, q, 1)
                    spread_sj(p, q)
                if q in RAW and k >= 6:
                    transpose_c(p, q, 2)
                    spread_r2(p, q)
                    spread_r1(p, q)
                if k < 6:
                    second_half(p, k, 0, q if q in RAW else None)
                    for f in range(FT):
                        hidden(p, k, 1, f)
                    second_half(p, k, 1)
                if k == 7:
                    pe.wait_ge(w_ready, 48)

            pe.wait_ge(const_ready, 19)
            pe.wait_ge(w_zero, 2)
            pe.wait_ge(raw_ready, 16 * (1 + 1 + 1 + 1 + 6))
            pe.transpose(TH[:, 0, 0:LAYERS * FT], b1rows, ident[0:LAYERS * FT, 0:LAYERS * FT])\
              .then_inc(b1t_done, 1)
            for jt in range(NT):
                transpose_mask(START, 8, jt)
            transpose_c(START, 8, 1)
            spread_sj(START, 8)
            transpose_c(START, 8, 2)
            spread_r2(START, 8)
            spread_r1(START, 8)
            pe.wait_ge(w_split, 2 * LAYERS)
            with pe.Fori(0, PAIRS) as p:
                for k in range(8):
                    step(p, k)
                pair_end(pe, "pe")


_INS = ['x', 'adj', 'L0_gnn_attn_w', 'L0_gnn_attn_b', 'L0_gnn_W1', 'L0_gnn_b1', 'L0_gnn_W2',
        'L0_gnn_b2', 'L0_gnn_g1', 'L0_gnn_beta1', 'L0_gnn_g2', 'L0_gnn_beta2', 'L1_gnn_W', 'L1_gnn_a']


def kernel(**inputs):
    import numpy as _np
    import concourse.bacc as _bacc
    from concourse import mybir as _mybir
    from concourse.bass_utils import run_bass_kernel_spmd as _run

    nc = _bacc.Bacc("TRN2", target_bir_lowering=False, num_devices=1)
    arrays, args = {}, []
    for name in _INS:
        a = _np.ascontiguousarray(inputs[name])
        arrays[f"in_{name}"] = a
        args.append(nc.dram_tensor(f"in_{name}", a.shape, _mybir.dt.from_np(a.dtype),
                                   kind="ExternalInput").ap())
    out = nc.dram_tensor("out_x", (BATCH, N, D), _mybir.dt.float32, kind="ExternalOutput").ap()
    build(nc, *args, out)
    r = _run(nc, [arrays], core_ids=[0])
    return r.results[0]["out_x"]
```
